# Optimizing a Trainium2 kernel written in Bass

```python
import numpy as np
import jax
import jax.numpy as jnp

def _softmax(x, axis=-1):
    return jax.nn.softmax(x, axis=axis)

def _gelu(x):
    return jax.nn.gelu(x, approximate=True)

def _silu(x):
    return jax.nn.silu(x)

def _sigmoid(x):
    return jax.nn.sigmoid(x)

def _layernorm(x, axis=-1, eps=1e-05):
    m = jnp.mean(x, axis=axis, keepdims=True)
    v = jnp.var(x, axis=axis, keepdims=True)
    return (x - m) / jnp.sqrt(v + eps)

def _scatter_add(tgt, idx, src, axis=0):
    return tgt.at[idx].add(src)

def _segment_sum(src, seg, n):
    return jax.ops.segment_sum(src, seg, n)
kernel_name = 'mk_recurrent_d1_jaxref_r4_e9a0b2'

def setup_inputs(seed: int=0):
    np.random.seed(seed)
    _w = jnp.asarray

    def _L0_attn_setup():
        import jax, jax.numpy as jnp
        import numpy as np
        from jax import lax
        D_MODEL = 256
        DEPTH = 8
        D_STATE = 16
        D_CONV = 4
        EXPAND = 2
        D_INNER = EXPAND * D_MODEL
        DT_RANK = (D_MODEL + 15) // 16
        B_SZ = 2
        SEQ = 512

        def _silu(v):
            return v * jax.nn.sigmoid(v)

        def _causal_conv(u, w, b):
            K = w.shape[-1]
            L = u.shape[1]
            up = jnp.pad(u, ((0, 0), (K - 1, 0), (0, 0)))
            y = sum((up[:, k:k + L, :] * w[:, k] for k in range(K)))
            return y + b

        def _selective_scan(delta, Bm, Cm, u, A, Dp):

            def step(h, inp):
                d_t, B_t, C_t, u_t = inp
                h = h * jnp.exp(d_t[..., None] * A) + (d_t * u_t)[..., None] * B_t[:, None, :]
                y = jnp.einsum('bcn,bn->bc', h, C_t)
                return (h, y)
            h0 = jnp.zeros((u.shape[0], A.shape[0], A.shape[1]), u.dtype)
            xs = (jnp.swapaxes(delta, 0, 1), jnp.swapaxes(Bm, 0, 1), jnp.swapaxes(Cm, 0, 1), jnp.swapaxes(u, 0, 1))
            _, ys = lax.scan(step, h0, xs)
            return jnp.swapaxes(ys, 0, 1) + u * Dp

        def _mamba_layer(x, Wi, cw, cb, Wx, Wdt, bdt, Alog, Dp, Wo):
            xz = jnp.einsum('bld,ed->ble', x, Wi)
            xin, z = jnp.split(xz, 2, axis=-1)
            xin = _silu(_causal_conv(xin, cw, cb))
            x_dbl = jnp.einsum('blc,ec->ble', xin, Wx)
            dt_raw = x_dbl[..., :DT_RANK]
            Bm = x_dbl[..., DT_RANK:DT_RANK + D_STATE]
            Cm = x_dbl[..., DT_RANK + D_STATE:]
            delta = jax.nn.softplus(jnp.einsum('blr,cr->blc', dt_raw, Wdt) + bdt)
            A = -jnp.exp(Alog)
            y = _selective_scan(delta, Bm, Cm, xin, A, Dp)
            y = y * _silu(z)
            return jnp.einsum('blc,dc->bld', y, Wo)
        key = jax.random.key(seed)
        ks = jax.random.split(key, 8)
        s = 0.02
        x = jax.random.normal(ks[0], (B_SZ, SEQ, D_MODEL), jnp.float32)
        W_in = jax.random.normal(ks[1], (DEPTH, 2 * D_INNER, D_MODEL), jnp.float32) * s
        conv_w = jax.random.normal(ks[2], (DEPTH, D_INNER, D_CONV), jnp.float32) * s
        conv_b = jnp.zeros((DEPTH, D_INNER), jnp.float32)
        W_x = jax.random.normal(ks[3], (DEPTH, DT_RANK + 2 * D_STATE, D_INNER), jnp.float32) * s
        W_dt = jax.random.normal(ks[4], (DEPTH, D_INNER, DT_RANK), jnp.float32) * s
        b_dt = jnp.full((DEPTH, D_INNER), -4.0, jnp.float32)
        A_log = jnp.tile(jnp.log(jnp.arange(1, D_STATE + 1, dtype=jnp.float32)), (DEPTH, D_INNER, 1))
        D_par = jnp.ones((DEPTH, D_INNER), jnp.float32)
        W_out = jax.random.normal(ks[5], (DEPTH, D_MODEL, D_INNER), jnp.float32) * s
        return {'x': x, 'W_in': W_in, 'conv_w': conv_w, 'conv_b': conv_b, 'W_x': W_x, 'W_dt': W_dt, 'b_dt': b_dt, 'A_log': A_log, 'D_par': D_par, 'W_out': W_out}
    _L0_attn_in = _L0_attn_setup()

    def _L0_ffn_setup():
        import jax, jax.numpy as jnp
        import numpy as np
        B, S, D, E, F = (2, 512, 256, 8, 1024)
        key = jax.random.key(seed)
        ks = jax.random.split(key, 4)
        return {'hidden_states': jax.random.normal(ks[0], (B, S, D), dtype=jnp.float32), 'Wr': jax.random.normal(ks[1], (D, E), dtype=jnp.float32) * (1.0 / np.sqrt(D)), 'W1': jax.random.normal(ks[2], (E, D, F), dtype=jnp.float32) * (1.0 / np.sqrt(D)), 'b1': jnp.zeros((E, F), dtype=jnp.float32), 'W2': jax.random.normal(ks[3], (E, F, D), dtype=jnp.float32) * (1.0 / np.sqrt(F)), 'b2': jnp.zeros((E, D), dtype=jnp.float32)}
    _L0_ffn_in = _L0_ffn_setup()
    _d = {'L0_attn_x': _L0_attn_in['x'], 'L0_attn_W_in': _L0_attn_in['W_in'], 'L0_attn_conv_w': _L0_attn_in['conv_w'], 'L0_attn_conv_b': _L0_attn_in['conv_b'], 'L0_attn_W_x': _L0_attn_in['W_x'], 'L0_attn_W_dt': _L0_attn_in['W_dt'], 'L0_attn_b_dt': _L0_attn_in['b_dt'], 'L0_attn_A_log': _L0_attn_in['A_log'], 'L0_attn_D_par': _L0_attn_in['D_par'], 'L0_attn_W_out': _L0_attn_in['W_out'], 'L0_ffn_Wr': _L0_ffn_in['Wr'], 'L0_ffn_W1': _L0_ffn_in['W1'], 'L0_ffn_b1': _L0_ffn_in['b1'], 'L0_ffn_W2': _L0_ffn_in['W2'], 'L0_ffn_b2': _L0_ffn_in['b2']}
    _x0 = _d['L0_attn_x']
    _d['L0_attn_x'] = jax.random.normal(jax.random.fold_in(jax.random.key(seed), 1), (4, 1024, 256), dtype=_x0.dtype)
    del _x0
    return _d

def reference(L0_attn_x, L0_attn_W_in, L0_attn_conv_w, L0_attn_conv_b, L0_attn_W_x, L0_attn_W_dt, L0_attn_b_dt, L0_attn_A_log, L0_attn_D_par, L0_attn_W_out, L0_ffn_Wr, L0_ffn_W1, L0_ffn_b1, L0_ffn_W2, L0_ffn_b2):

    def _L0_attn_ref(x, W_in, conv_w, conv_b, W_x, W_dt, b_dt, A_log, D_par, W_out):
        import jax, jax.numpy as jnp
        import numpy as np
        from jax import lax
        D_MODEL = 256
        DEPTH = 8
        D_STATE = 16
        D_CONV = 4
        EXPAND = 2
        D_INNER = EXPAND * D_MODEL
        DT_RANK = (D_MODEL + 15) // 16
        B_SZ = 2
        SEQ = 512

        def _silu(v):
            return v * jax.nn.sigmoid(v)

        def _causal_conv(u, w, b):
            K = w.shape[-1]
            L = u.shape[1]
            up = jnp.pad(u, ((0, 0), (K - 1, 0), (0, 0)))
            y = sum((up[:, k:k + L, :] * w[:, k] for k in range(K)))
            return y + b

        def _selective_scan(delta, Bm, Cm, u, A, Dp):

            def step(h, inp):
                d_t, B_t, C_t, u_t = inp
                h = h * jnp.exp(d_t[..., None] * A) + (d_t * u_t)[..., None] * B_t[:, None, :]
                y = jnp.einsum('bcn,bn->bc', h, C_t)
                return (h, y)
            h0 = jnp.zeros((u.shape[0], A.shape[0], A.shape[1]), u.dtype)
            xs = (jnp.swapaxes(delta, 0, 1), jnp.swapaxes(Bm, 0, 1), jnp.swapaxes(Cm, 0, 1), jnp.swapaxes(u, 0, 1))
            _, ys = lax.scan(step, h0, xs)
            return jnp.swapaxes(ys, 0, 1) + u * Dp

        def _mamba_layer(x, Wi, cw, cb, Wx, Wdt, bdt, Alog, Dp, Wo):
            xz = jnp.einsum('bld,ed->ble', x, Wi)
            xin, z = jnp.split(xz, 2, axis=-1)
            xin = _silu(_causal_conv(xin, cw, cb))
            x_dbl = jnp.einsum('blc,ec->ble', xin, Wx)
            dt_raw = x_dbl[..., :DT_RANK]
            Bm = x_dbl[..., DT_RANK:DT_RANK + D_STATE]
            Cm = x_dbl[..., DT_RANK + D_STATE:]
            delta = jax.nn.softplus(jnp.einsum('blr,cr->blc', dt_raw, Wdt) + bdt)
            A = -jnp.exp(Alog)
            y = _selective_scan(delta, Bm, Cm, xin, A, Dp)
            y = y * _silu(z)
            return jnp.einsum('blc,dc->bld', y, Wo)
        for i in range(DEPTH):
            x = x + _mamba_layer(x, W_in[i], conv_w[i], conv_b[i], W_x[i], W_dt[i], b_dt[i], A_log[i], D_par[i], W_out[i])
        return jnp.nan_to_num(x)

    def _L0_ffn_ref(hidden_states, Wr, W1, b1, W2, b2):
        import jax, jax.numpy as jnp
        import numpy as np
        B, S, D, E, F = (2, 512, 256, 8, 1024)
        b, s, d = hidden_states.shape
        e = Wr.shape[1]
        x = hidden_states.reshape(b * s, d)
        router_logits = x @ Wr
        router_probs = jax.nn.softmax(router_logits, axis=-1)
        expert_idx = jnp.argmax(router_probs, axis=-1)
        p_max = jnp.max(router_probs, axis=-1, keepdims=True)

        def expert_mlp(w1, bb1, w2, bb2):
            h = jax.nn.gelu(x @ w1 + bb1, approximate=False)
            return h @ w2 + bb2
        outs = jax.vmap(expert_mlp)(W1, b1, W2, b2)
        onehot = jax.nn.one_hot(expert_idx, e, dtype=x.dtype)
        next_states = jnp.einsum('te,etd->td', onehot, outs)
        out = p_max * next_states
        return out.reshape(b, s, d)
    x = L0_attn_x
    xn = _layernorm(x, axis=-1)
    s = _L0_attn_ref(xn, L0_attn_W_in, L0_attn_conv_w, L0_attn_conv_b, L0_attn_W_x, L0_attn_W_dt, L0_attn_b_dt, L0_attn_A_log, L0_attn_D_par, L0_attn_W_out)
    g = _silu(_L0_ffn_ref(xn, L0_ffn_Wr, L0_ffn_W1, L0_ffn_b1, L0_ffn_W2, L0_ffn_b2))
    x = x + s * g
    return x

_drawn_inputs = setup_inputs


def setup_inputs(seed=0):
    import zlib

    import numpy as np

    out = dict(_drawn_inputs(seed))
    spreads = {'L0_attn_conv_b': (0.0, 0.8),
     'L0_attn_b_dt': (-4.0, 0.6),
     'L0_attn_D_par': (1.0, 0.6),
     'L0_ffn_b1': (0.0, 0.578),
     'L0_ffn_b2': (0.0, 0.398)}
    factors = {'L0_attn_W_in': 8.0,
     'L0_attn_conv_w': 8.0,
     'L0_attn_W_x': 8.0,
     'L0_attn_W_dt': 8.0,
     'L0_attn_A_log': 8.0,
     'L0_attn_W_out': 8.0}
    for name, (base, spread) in spreads.items():
        noise = np.random.default_rng([zlib.crc32(name.encode()), seed]).standard_normal(out[name].shape)
        drawn = base * np.exp(spread * noise) if base else spread * noise
        out[name] = jnp.asarray(drawn.astype(out[name].dtype))
    for name, factor in factors.items():
        out[name] = (out[name] * factor).astype(out[name].dtype)
    return out
```

```python
from contextlib import ExitStack

import numpy as np
import concourse.bass as bass
from concourse import mybir

F32 = mybir.dt.float32
ALU = mybir.AluOpType
ACT = mybir.ActivationFunctionType
AX_X = mybir.AxisListType.X

P = 128
LAYERS, BATCH, SEQ, D = 8, 4, 1024, 256
INNER, STATES, TAPS, RANK = 512, 16, 4, 16
TOK = BATCH * SEQ
T = 512
TC = T // P
CB = INNER // P
DB = D // P
HALVES = SEQ // T
ITERS = LAYERS * BATCH
UPL = BATCH * HALVES
EXPERTS, FF = 8, 1024
FB = FF // P
NTILE = TOK // P
EPS = 1e-5
FLT_MAX = float(np.finfo(np.float32).max)
LIMIT = 1e7

ON_GPSIMD = [2, 5, 7, 10, 13]
ON_VECTOR = [n for n in range(STATES) if n not in ON_GPSIMD]
NV, NG = len(ON_VECTOR), len(ON_GPSIMD)

COL_A = 0
COL_W = COL_A + CB * STATES
COL_CB = COL_W + CB * TAPS
COL_DT = COL_CB + CB
COL_D = COL_DT + CB
NPAR = COL_D + CB

X_IN, Z_IN, DT_RAW, BC_IN, DT_IN, DU_T = 0, CB, 2 * CB, 2 * CB + 1, 2 * CB + 2, 3 * CB + 2
FRONT = DU_T + TC
FRONT_BANKS = 3
assert FRONT % FRONT_BANKS == 0
FRONT_ACT, FRONT_VEC = FRONT - CB, CB
BACK = CB + DB

SCAN_0 = CB
DBU_0 = 2 * CB
HT_0 = 2 * TC
BACK_0 = BACK * UPL


def act_reads(U, item):
    return FRONT_ACT * (U + 1) + item + 1 - (CB if item >= Z_IN + CB else 0)


def vec_reads(U, j):
    return FRONT_VEC * (U + 1) + j + 1


def normalise(nc, x, xn_dram, xres, ident):
    with ExitStack() as ctx:
        sb = lambda name, shape: ctx.enter_context(nc.sbuf_tensor(name, shape, F32))
        sem = lambda name: ctx.enter_context(nc.semaphore(name))
        xt = sb("ln_x", [P, NTILE, D])
        stats = sb("ln_stats", [P, NTILE, nc.vector.BN_STATS_DIM])
        mv = sb("ln_mv", [P, NTILE, 2])
        std = sb("ln_std", [P, NTILE])
        rstd = sb("ln_rstd", [P, NTILE])
        eps = sb("ln_eps", [P, 1])
        ps = ctx.enter_context(nc.psum_tensor("ln_ps", [P, 4, 512], F32))
        x_in, id_set, stats_done, mv_done = sem("x_in"), sem("id_set"), sem("stats_done"), sem("mv_done")
        eps_set, std_done, rstd_done = sem("eps_set"), sem("std_done"), sem("rstd_done")
        xn_done, turned, kept, xn_out = sem("xn_done"), sem("turned"), sem("kept"), sem("xn_out")
        block = ctx.enter_context(nc.Block())

        @block.sync
        def _(sp):
            sp.dma_start(xt[:], x.rearrange("(i p) d -> p i d", p=P)).then_inc(x_in, 16)
            sp.wait_ge(kept, NTILE)
            sp.dma_start(xn_dram, xres[:]).then_inc(xn_out, 16)
            sp.wait_ge(xn_out, 16)

        @block.gpsimd
        def _(pool):
            nc.gpsimd.memset(ident[:], 0.0).then_inc(id_set, 1)
            pool.wait_ge(id_set, 1)
            nc.gpsimd.affine_select(out=ident[:], in_=ident[:], compare_op=ALU.not_equal, fill=1.0,
                                    base=0, pattern=[[-1, P]], channel_multiplier=1).then_inc(id_set, 1)

        @block.vector
        def _(dve):
            nc.vector.memset(eps[:], EPS).then_inc(eps_set, 1)
            dve.wait_ge(x_in, 16)
            for i in range(NTILE):
                nc.vector.bn_stats(stats[:, i, :], xt[:, i, :]).then_inc(stats_done, 1)
            for i in range(NTILE):
                dve.wait_ge(stats_done, i + 1)
                nc.vector.bn_aggr(mv[:, i, :], stats[:, i, :]).then_inc(mv_done, 1)
            dve.wait_ge(std_done, 1)
            nc.vector.reciprocal(rstd[:], std[:]).then_inc(rstd_done, 1)
            dve.wait_ge(rstd_done, 1)
            for i in range(NTILE):
                nc.vector.tensor_scalar(xt[:, i, :], xt[:, i, :], mv[:, i, 0:1], rstd[:, i:i + 1],
                                        ALU.subtract, ALU.mult).then_inc(xn_done, 1)

        @block.scalar
        def _(act):
            act.wait_ge(eps_set, 1)
            act.wait_ge(mv_done, NTILE)
            nc.scalar.activation(std[:], mv[:, :, 1], ACT.Sqrt, bias=eps[:, 0:1]).then_inc(std_done, 1)
            for i in range(NTILE):
                act.wait_ge(turned, i + 1)
                nc.scalar.activation(xres[:, :, i * P:(i + 1) * P],
                                     ps[:, i % 4, 0:D].rearrange("p (k t) -> p k t", k=DB),
                                     ACT.Copy).then_inc(kept, 1)

        @block.tensor
        def _(pe):
            pe.wait_ge(id_set, 2)
            for i in range(NTILE):
                pe.wait_ge(xn_done, i + 1)
                if i >= 4:
                    pe.wait_ge(kept, i - 3)
                for k in range(DB):
                    last = nc.tensor.transpose(ps[:, i % 4, k * P:(k + 1) * P], xt[:, i, k * P:(k + 1) * P], ident[:])
                last.then_inc(turned, 1)


def mamba(nc, w_in, w_x, w_dt, w_out, par, xres, ident, alive_dram):
    with ExitStack() as ctx:
        sb = lambda name, shape: ctx.enter_context(nc.sbuf_tensor(name, shape, F32))
        sem = lambda name: ctx.enter_context(nc.semaphore(name))
        w_in_sb = sb("w_in_sb", [P, DB, 2 * INNER])
        w_x_sb = sb("w_x_sb", [P, CB, RANK + 2 * STATES])
        w_dt_sb = sb("w_dt_sb", [RANK, INNER])
        w_out_sb = sb("w_out_sb", [P, CB, D])
        params = sb("params", [P, LAYERS, NPAR])
        cur = [sb(f"cur{h}", [P, NPAR]) for h in range(2)]
        u = [sb(f"u{h}", [P, CB, T]) for h in range(2)]
        zs = [sb(f"zs{h}", [P, CB, T]) for h in range(2)]
        delta = [sb(f"delta{h}", [P, CB, T]) for h in range(2)]
        duT = sb("duT", [P, TC, INNER])
        bc = [sb(f"bc{h}", [P, TC * 2 * STATES]) for h in range(2)]
        xm = sb("xm", [P, DB, T])
        alive = sb("alive", [P, T])
        dead = sb("dead", [P, 1])
        ones_mat = sb("ones_mat", [P, P])
        zeros = sb("zeros", [P, 1])
        xpad = sb("xpad", [P, CB, TAPS - 1 + T])
        th = sb("th", [P, CB, T])
        relu = th
        gated = th
        soft = sb("soft", [P, CB, T])
        du = soft
        low = sb("low", [P, 2, T])
        dt_raw = sb("dt_raw", [RANK, T])
        duB = [sb(f"duB{k}", [P, TC, INNER]) for k in range(2)]
        decay = sb("decay", [P, SCAN_0, T])
        state = [sb(f"state{k}", [P, CB, T]) for k in range(2)]
        carry = sb("carry", [P, STATES, CB])
        yv = sb("yv", [P, TC, INNER])
        yg = sb("yg", [P, TC, INNER])
        prod = sb("prod", [P, 2, INNER])
        ps_b = ctx.enter_context(nc.psum_tensor("ps_b", [P, 2, T], F32))
        ps_s = ctx.enter_context(nc.psum_tensor("ps_s", [P, 2, INNER], F32))
        ps_f = ctx.enter_context(nc.psum_tensor("ps_f", [P, FRONT_BANKS, 512], F32))
        ps_k = ctx.enter_context(nc.psum_tensor("ps_k", [P, 512], F32))

        par_in, par_set = sem("par_in"), sem("par_set")
        w_in_in, w_x_in, w_out_in = sem("w_in_in"), sem("w_x_in"), sem("w_out_in")
        front_ready, front_act, front_vec = sem("front_ready"), sem("front_act"), sem("front_vec")
        halo_set, xpad_set, conv_step, conv_done = sem("halo_set"), sem("xpad_set"), sem("conv_step"), sem("conv_done")
        th_set, u_done = sem("th_set"), sem("u_done")
        exp_done, log_done, soft_step = sem("exp_done"), sem("log_done"), sem("soft_step")
        delta_done = sem("delta_done")
        over_part = sem("over_part")
        over_set, over_counted, over_read, dead_set = sem("over_set"), sem("over_counted"), sem("over_read"), sem("dead_set")
        alive_set, alive_out, xm_set = sem("alive_set"), sem("alive_out"), sem("xm_set")
        par_exp, pool_waited = sem("par_exp"), sem("pool_waited")
        cur_set, duB_done, duB_turned, decay_done = sem("cur_set"), sem("duB_done"), sem("duB_turned"), sem("decay_done")
        scanned, state_turned, carried = sem("scanned"), sem("state_turned"), sem("carried")
        yv_added, prod_done, yg_added, y_done = sem("yv_added"), sem("prod_done"), sem("yg_added"), sem("y_done")
        back_ready, back_read, gated_done = sem("back_ready"), sem("back_read"), sem("gated_done")
        block = ctx.enter_context(nc.Block())

        def units(eng, unit):
            with eng.Fori(0, ITERS - 1) as it:
                for h in range(HALVES):
                    unit(HALVES * it + h, h, it, True)
            for h in range(HALVES):
                unit(HALVES * (ITERS - 1) + h, h, ITERS - 1, h + 1 < HALVES)

        @block.sync
        def _(sp):
            sp.dma_start(params[:], par).then_inc(par_in, 16)

            def store_alive(U, h, it):
                sp.wait_ge(alive_set, U + 1)
                sp.dma_start(alive_dram[:, bass.ds((it % BATCH) * SEQ + h * T, T)], alive[0:1, :]).then_inc(alive_out, 16)

            def load_in(layer):
                sp.dma_start(w_in_sb[:], w_in[:, :, bass.ds(layer * 2 * INNER, 2 * INNER)]).then_inc(w_in_in, 16)

            def load_x(layer):
                sp.dma_start(w_x_sb[:], w_x[:, :, bass.ds(layer * (RANK + 2 * STATES), RANK + 2 * STATES)]).then_inc(w_x_in, 16)
                sp.dma_start(w_dt_sb[:], w_dt[:, bass.ds(layer * INNER, INNER)]).then_inc(w_x_in, 16)

            def load_out(layer):
                sp.dma_start(w_out_sb[:], w_out[:, :, bass.ds(layer * D, D)]).then_inc(w_out_in, 16)

            def stores(layer):
                for b in range(BATCH):
                    for h in range(HALVES):
                        store_alive((layer * BATCH + b) * HALVES + h, h, b)

            load_in(0)
            load_x(0)
            load_out(0)
            with sp.Fori(1, LAYERS) as layer:
                stores(layer - 1)
                sp.wait_ge(front_ready, (layer * UPL - 1) * FRONT + Z_IN + CB)
                load_in(layer)
                sp.wait_ge(front_ready, (layer * UPL - 1) * FRONT + DT_IN + CB)
                load_x(layer)
                sp.wait_ge(back_ready, layer * UPL * BACK)
                load_out(layer)
            stores(LAYERS - 1)
            sp.wait_ge(alive_out, 16 * LAYERS * UPL)

        @block.gpsimd
        def _(pool):
            def wait_counted(semaphore, count):
                pool.wait_ge(semaphore, count)
                pool.sem_inc(pool_waited, 1)

            def unit(U, h, it, more):
                for n in range(STATES + 2):
                    if n < STATES:
                        for t in range(TC):
                            if n == 0:
                                wait_counted(front_act, act_reads(U, DU_T + t))
                            if t == 0:
                                wait_counted(duB_turned, U * STATES * CB + CB * n + CB)
                            nc.gpsimd.tensor_scalar(duB[n % 2][:, t, :], duT[:, t, :],
                                                    bc[h][:, t * 2 * STATES + n:t * 2 * STATES + n + 1], 1.0,
                                                    ALU.mult, ALU.mult).then_inc(duB_done, 1)
                    if n - 2 in ON_GPSIMD[1:]:
                        g = ON_GPSIMD.index(n - 2)
                        for t in range(TC):
                            pool.wait_ge(prod_done, U * TC * NG + TC * g + t + 1)
                            if g > 1:
                                pool.wait_ge(yg_added, U * TC * (NG - 1) + TC * (g - 2) + t + 1)
                            nc.gpsimd.tensor_tensor(yg[:, t, :], yg[:, t, :], prod[:, t % 2, :], ALU.add).then_inc(yg_added, 1)

            units(pool, unit)

        @block.scalar
        def _(act):
            def copy_x(U, j):
                act.wait_ge(front_ready, U * FRONT + X_IN + j + 1)
                act.wait_ge(halo_set, U + 1)
                nc.scalar.activation(xpad[:, j, TAPS - 1:], ps_f[:, (X_IN + j) % FRONT_BANKS, :], ACT.Copy).then_inc(front_act, 1)

            def tanh_z(U, j):
                act.wait_ge(front_ready, U * FRONT + Z_IN + j + 1)
                act.wait_ge(u_done, CB * U + j + 1)
                nc.scalar.activation(th[:, j, :], ps_f[:, (Z_IN + j) % FRONT_BANKS, :], ACT.Tanh, scale=0.5).then_inc(th_set, 1)

            def tanh_u(U, h, j):
                act.wait_ge(conv_done, CB * U + j + 1)
                act.wait_ge(front_vec, vec_reads(U, j))
                nc.scalar.activation(th[:, j, :], u[h][:, j, :], ACT.Tanh).then_inc(th_set, 1)

            def copy_dt_bc(U, h):
                act.wait_ge(front_ready, U * FRONT + DT_RAW + 1)
                nc.scalar.activation(dt_raw[:], ps_f[0:RANK, DT_RAW % FRONT_BANKS, :], ACT.Copy).then_inc(front_act, 1)
                act.wait_ge(front_ready, U * FRONT + BC_IN + 1)
                nc.scalar.activation(bc[h][:], ps_f[:, BC_IN % FRONT_BANKS, 0:TC * 2 * STATES], ACT.Copy).then_inc(front_act, 1)

            def relu_abs(U, h, j):
                bias = cur[h][:, COL_DT + j:COL_DT + j + 1]
                act.wait_ge(front_ready, U * FRONT + DT_IN + j + 1)
                act.wait_ge(cur_set, U + 1)
                act.wait_ge(u_done, CB * U + 2 * CB)
                if j == 0:
                    act.wait_ge(front_ready, U * FRONT + 1)
                nc.scalar.activation(relu[:, j, :], ps_f[:, (DT_IN + j) % FRONT_BANKS, :], ACT.Relu, bias=bias)
                nc.scalar.activation(soft[:, j, :], ps_f[:, (DT_IN + j) % FRONT_BANKS, :], ACT.Abs, bias=bias).then_inc(front_act, 1)

            def exponential(U):
                act.wait_ge(front_act, act_reads(U, DT_IN + CB - 1))
                nc.scalar.activation(soft[:], soft[:], ACT.Exp, scale=-1.0).then_inc(exp_done, 1)

            def logarithm(U, h):
                act.wait_ge(exp_done, U + 1)
                nc.scalar.activation(delta[h][:], soft[:], ACT.Ln, bias=1.0).then_inc(log_done, 1)

            def copy_duT(U, h, t):
                act.wait_ge(front_ready, U * FRONT + DU_T + t + 1)
                if t == 0 and not (isinstance(U, int) and U == 0):
                    act.wait_ge(duB_done, U * STATES * TC)
                nc.scalar.activation(duT[:, t, :], ps_f[:, (DU_T + t) % FRONT_BANKS, :], ACT.Copy).then_inc(front_act, 1)

            def front(U, h, n):
                if n == 2:
                    copy_x(U, 0)
                if n == 3:
                    copy_x(U, 1)
                    copy_x(U, 2)
                if n == 4:
                    copy_x(U, 3)
                    tanh_z(U, 0)
                if n == 5:
                    tanh_z(U, 1)
                if n == 6:
                    tanh_z(U, 2)
                    tanh_z(U, 3)
                if n in (7, 8):
                    tanh_u(U, h, 2 * (n - 7))
                    tanh_u(U, h, 2 * (n - 7) + 1)
                if n == 9:
                    copy_dt_bc(U, h)
                if n in (10, 11):
                    relu_abs(U, h, 2 * (n - 10))
                    relu_abs(U, h, 2 * (n - 10) + 1)
                if n == 11:
                    exponential(U)
                if n in (15, 16):
                    copy_duT(U, h, 2 * (n - 15))
                    copy_duT(U, h, 2 * (n - 15) + 1)

            def unit(U, h, it, more):
                for n in range(STATES + 1):
                    if n < STATES:
                        for j in range(CB):
                            if n == 0 and j == 0:
                                act.wait_ge(delta_done, U + 2)
                            act.wait_ge(scanned, U * STATES * CB + CB * n + j + 1)
                            a = COL_A + j * STATES + n
                            nc.scalar.activation(decay[:, j, :], delta[h][:, j, :], ACT.Exp,
                                                 scale=cur[h][:, a:a + 1]).then_inc(decay_done, 1)
                    if more and n == 12:
                        logarithm(U + 1, 1 - h)
                    if n - 1 in ON_GPSIMD:
                        g = ON_GPSIMD.index(n - 1)
                        for t in range(TC):
                            c = t * 2 * STATES + STATES + n - 1
                            act.wait_ge(state_turned, HT_0 + U * STATES * TC + TC * (n - 1) + t + 1)
                            if g == 0:
                                act.wait_ge(y_done, TC * U + t + 1)
                            elif g > 1 or t >= 2:
                                act.wait_ge(yg_added, U * TC * (NG - 1) + TC * (g - 1) + t - 1)
                            nc.scalar.activation(yg[:, t, :] if g == 0 else prod[:, t % 2, :], ps_s[:, t % 2, :], ACT.Copy,
                                                 scale=bc[h][:, c:c + 1]).then_inc(prod_done, 1)
                    if more:
                        front(U + 1, 1 - h, n)

            act.sem_inc(front_act, FRONT_ACT)
            act.wait_ge(par_in, 16)
            nc.scalar.activation(params[:, :, COL_A:COL_W], params[:, :, COL_A:COL_W], ACT.Exp).then_inc(par_exp, 1)
            for n in range(STATES + 1):
                if n == 12:
                    logarithm(0, 0)
                front(0, 0, n)
            units(act, unit)

        @block.vector
        def _(dve):
            def set_cur(U, h, layer):
                nc.vector.tensor_copy(cur[h][:], params[:, bass.ds(layer, 1), :].rearrange("p a c -> p (a c)")).then_inc(cur_set, 1)

            def mark_over(U, h, it):
                xs = xres[:, :, bass.ds((it % BATCH) * SEQ + h * T, T)]
                nc.vector.tensor_scalar(xm[:], xs, LIMIT, None, ALU.is_gt).then_inc(over_part, 1)
                dve.wait_ge(over_part, U + 1)
                nc.vector.scalar_tensor_tensor(xm[:], xs, -LIMIT, xm[:], ALU.is_lt, ALU.add).then_inc(over_set, 1)

            def mask_x(U, h, it):
                dve.wait_ge(over_counted, U + 1)
                dve.wait_ge(dead_set, U + 1)
                if not (isinstance(U, int) and U == 0):
                    dve.wait_ge(alive_out, 16 * U)
                nc.vector.tensor_tensor_scan(alive[:], ps_k[:], zeros[:, 0:1].to_broadcast([P, T]), dead[:, 0:1], ALU.max, ALU.max).then_inc(over_read, 1)
                dve.wait_ge(over_read, U + 1)
                if h == 0:
                    nc.vector.tensor_copy(dead[:], alive[:, T - 1:T]).then_inc(dead_set, 1)
                else:
                    nc.vector.memset(dead[:], 0.0).then_inc(dead_set, 1)
                dve.wait_ge(dead_set, U + 2)
                nc.vector.tensor_scalar(alive[:], alive[:], 0.5, None, ALU.is_lt).then_inc(alive_set, 1)
                dve.wait_ge(alive_set, U + 1)
                nc.vector.tensor_tensor(xm[:], xres[:, :, bass.ds((it % BATCH) * SEQ + h * T, T)],
                                        alive[:].unsqueeze(1).to_broadcast([P, DB, T]), ALU.mult).then_inc(xm_set, 1)

            def conv(U, h, blocks):
                for k in range(TAPS):
                    tap = TAPS - 1 - k
                    for i, j in enumerate(blocks):
                        w = cur[h][:, COL_W + j * TAPS + tap:COL_W + j * TAPS + tap + 1]
                        if k == 0:
                            dve.wait_ge(cur_set, U + 1)
                            dve.wait_ge(front_act, act_reads(U, X_IN + j))
                            step = nc.vector.tensor_scalar(u[h][:, j, :], xpad[:, j, tap:tap + T], w,
                                                           cur[h][:, COL_CB + j:COL_CB + j + 1], ALU.mult, ALU.add)
                        else:
                            dve.wait_ge(conv_step, (TAPS - 1) * (CB * U + blocks[0]) + (k - 1) * len(blocks) + i + 1)
                            step = nc.vector.scalar_tensor_tensor(u[h][:, j, :], xpad[:, j, tap:tap + T], w,
                                                                  u[h][:, j, :], ALU.mult, ALU.add)
                        step.then_inc(conv_done if k == TAPS - 1 else conv_step, 1)

            def halo(U, h):
                dve.wait_ge(conv_done, CB * U + CB)
                if h == 0:
                    nc.vector.tensor_copy(xpad[:, :, 0:TAPS - 1], xpad[:, :, T:T + TAPS - 1]).then_inc(halo_set, 1)
                else:
                    nc.vector.memset(xpad[:, :, 0:TAPS - 1], 0.0).then_inc(halo_set, 1)

            def silu_z(U, h, j):
                dve.wait_ge(th_set, 2 * CB * U + j + 1)
                nc.vector.scalar_tensor_tensor(zs[h][:, j, :], th[:, j, :], 1.0, ps_f[:, (Z_IN + j) % FRONT_BANKS, :],
                                               ALU.add, ALU.mult).then_inc(front_vec, 1)

            def silu_u(U, h, j):
                dve.wait_ge(th_set, 2 * CB * U + CB + j + 1)
                nc.vector.scalar_tensor_tensor(u[h][:, j, :], th[:, j, :], 1.0, u[h][:, j, :],
                                               ALU.add, ALU.mult).then_inc(u_done, 1)

            def softplus(U, h, pair):
                dve.wait_ge(log_done, U + 1)
                blocks = [pair, pair + 1]
                for j in blocks:
                    nc.vector.tensor_scalar(low[:, j % 2, :], soft[:, j, :], 1.0, 1.0, ALU.add, ALU.subtract).then_inc(soft_step, 1)
                for j in blocks:
                    dve.wait_ge(soft_step, 4 * CB * U + 4 * pair + j % 2 + 1)
                    nc.vector.tensor_tensor(low[:, j % 2, :], soft[:, j, :], low[:, j % 2, :], ALU.subtract).then_inc(soft_step, 1)
                for j in blocks:
                    dve.wait_ge(soft_step, 4 * CB * U + 4 * pair + 2 + j % 2 + 1)
                    nc.vector.tensor_tensor(low[:, j % 2, :], low[:, j % 2, :], delta[h][:, j, :], ALU.add).then_inc(soft_step, 1)
                for j in blocks:
                    dve.wait_ge(soft_step, 4 * CB * U + 4 * pair + 4 + j % 2 + 1)
                    nc.vector.tensor_tensor(delta[h][:, j, :], low[:, j % 2, :], relu[:, j, :], ALU.add).then_inc(soft_step, 1)
                dve.wait_ge(soft_step, 4 * CB * U + 4 * pair + 8)
                for j in blocks:
                    last = nc.vector.tensor_tensor(du[:, j, :], delta[h][:, j, :], u[h][:, j, :], ALU.mult)
                if pair == CB - 2:
                    last.then_inc(delta_done, 1)

            def front(U, h, n, it):
                if n == 2:
                    set_cur(U, h, it // BATCH)
                if n == 4:
                    conv(U, h, [0, 1])
                if n == 5:
                    silu_z(U, h, 0)
                    conv(U, h, [2, 3])
                    halo(U, h)
                    silu_z(U, h, 1)
                if n in (6, 7):
                    silu_z(U, h, n - 4)
                if n == 8:
                    for j in range(CB):
                        silu_u(U, h, j)
                if n in (13, 14):
                    softplus(U, h, 2 * (n - 13))

            def scan(U, h, it, n, j):
                dve.wait_ge(decay_done, U * STATES * CB + CB * n + j + 1)
                dve.wait_ge(duB_turned, DBU_0 + U * STATES * CB + CB * n + j + 1)
                if j == 0:
                    dve.wait_ge(state_turned, U * STATES * TC + TC * n + TC)
                    if h == 1 and n == 0:
                        dve.wait_ge(carried, STATES * (it + 1))
                nc.vector.tensor_tensor_scan(state[n % 2][:, j, :], decay[:, j, :], ps_b[:, j % 2, :],
                                             carry[:, n, j:j + 1] if h == 1 else 0.0, ALU.mult, ALU.add).then_inc(scanned, 1)

            def add_y(U, h, n, t):
                if n not in ON_VECTOR:
                    return
                v = ON_VECTOR.index(n)
                c = t * 2 * STATES + STATES + n
                dve.wait_ge(state_turned, HT_0 + U * STATES * TC + TC * n + t + 1)
                if v == 0:
                    nc.vector.tensor_scalar(yv[:, t, :], ps_s[:, t % 2, :], bc[h][:, c:c + 1], None,
                                            ALU.mult).then_inc(yv_added, 1)
                else:
                    dve.wait_ge(yv_added, (U + 1) * TC * NV + TC * (v - 1) + t + 1)
                    nc.vector.scalar_tensor_tensor(yv[:, t, :], ps_s[:, t % 2, :], bc[h][:, c:c + 1], yv[:, t, :],
                                                   ALU.mult, ALU.add).then_inc(yv_added, 1)

            def sum_y(U):
                for t in range(TC):
                    dve.wait_ge(yv_added, (U + 1) * TC * NV + TC * (NV - 1) + t + 1)
                    dve.wait_ge(yg_added, U * TC * (NG - 1) + TC * (NG - 2) + t + 1)
                    nc.vector.tensor_tensor(yv[:, t, :], yv[:, t, :], yg[:, t, :], ALU.add).then_inc(y_done, 1)

            def gate(U, h, j):
                dve.wait_ge(back_ready, BACK * U + j + 1)
                nc.vector.scalar_tensor_tensor(gated[:, j, :], u[h][:, j, :], cur[h][:, COL_D + j:COL_D + j + 1],
                                               ps_k[:], ALU.mult, ALU.add).then_inc(back_read, 1)
                dve.wait_ge(back_read, BACK_0 + BACK * U + j + 1)
                nc.vector.scalar_tensor_tensor(gated[:, j, :], gated[:, j, :], 0.5, zs[h][:, j, :],
                                               ALU.mult, ALU.mult).then_inc(gated_done, 1)

            def add_x(U, h, it, k):
                xs = xres[:, k, bass.ds((it % BATCH) * SEQ + h * T, T)]
                dve.wait_ge(back_ready, BACK * U + CB + k + 1)
                nc.vector.tensor_tensor(xs, xs, ps_k[:], ALU.add).then_inc(back_read, 1)

            def unit(U, h, it, more):
                for n in range(STATES + 1):
                    if n == 0 and more:
                        mark_over(U + 1, 1 - h, it + h)
                    for j in range(CB):
                        if n < STATES:
                            scan(U, h, it, n, j)
                        if n == 0 and j == 0 and more:
                            mask_x(U + 1, 1 - h, it + h)
                        if n == 0 and h == 1:
                            gate(U - 1, 0, j)
                        if n and j:
                            add_y(U, h, n - 1, j - 1)
                        if h == 0 and n and j == 1:
                            dve.wait_ge(scanned, SCAN_0 + U * STATES * CB + CB * n)
                            nc.vector.tensor_copy(carry[:, n - 1, :], state[(n - 1) % 2][:, :, T - 1]).then_inc(carried, 1)
                    if n:
                        add_y(U, h, n - 1, TC - 1)
                    if n in (1, 2) and h == 1:
                        add_x(U - 1, 0, it, n - 1)
                    if more:
                        front(U + 1, 1 - h, n, it + h)
                sum_y(U)
                if h == 1:
                    for j in range(CB):
                        gate(U, 1, j)
                    for k in range(DB):
                        add_x(U, 1, it, k)

            dve.sem_inc(u_done, CB)
            dve.sem_inc(front_vec, FRONT_VEC)
            dve.sem_inc(delta_done, 1)
            dve.sem_inc(scanned, SCAN_0)
            dve.sem_inc(yv_added, TC * NV)
            dve.sem_inc(y_done, TC)
            dve.sem_inc(back_read, BACK_0)
            nc.vector.memset(xpad[:, :, 0:TAPS - 1], 0.0).then_inc(halo_set, 1)
            nc.vector.memset(dead[:], 0.0).then_inc(dead_set, 1)
            nc.vector.memset(zeros[:], 0.0)
            nc.vector.memset(ones_mat[:], 1.0)
            dve.wait_ge(par_in, 16)
            nc.vector.tensor_scalar(params[:, :, COL_W:COL_DT], params[:, :, COL_W:COL_DT], 0.5, None, ALU.mult).then_inc(par_set, 1)
            dve.wait_ge(par_exp, 1)
            nc.vector.tensor_scalar(params[:, :, COL_A:COL_W], params[:, :, COL_A:COL_W], -1.0, None, ALU.mult).then_inc(par_set, 1)
            dve.wait_ge(par_set, 2)
            mark_over(0, 0, 0)
            mask_x(0, 0, 0)
            for n in range(STATES + 1):
                front(0, 0, n, 0)
            units(dve, unit)

        @block.tensor
        def _(pe):
            def bank(U, item):
                before = item - FRONT_BANKS
                if before < 0:
                    pe.wait_ge(front_act, act_reads(U, before + FRONT) - FRONT_ACT)
                elif Z_IN <= before < Z_IN + CB:
                    pe.wait_ge(front_vec, vec_reads(U, before - Z_IN))
                else:
                    pe.wait_ge(front_act, act_reads(U, before))
                return ps_f[:, item % FRONT_BANKS, :]

            def count_over(U, h):
                pe.wait_ge(over_set, U + 1)
                pe.wait_ge(back_read, BACK_0 + BACK * U - (BACK if h == 1 else 2 * BACK))
                for k in range(DB):
                    last = nc.tensor.matmul(ps_k[:], ones_mat[:], xm[:, k, :], start=(k == 0), stop=(k == DB - 1))
                last.then_inc(over_counted, 1)

            def in_proj(U, h, it, item):
                if item == X_IN:
                    pe.wait_ge(w_in_in, 16 * (it // BATCH) + 16)
                    pe.wait_ge(xm_set, U + 1)
                out = bank(U, item)
                for k in range(DB):
                    last = nc.tensor.matmul(out, w_in_sb[:, k, item * P:(item + 1) * P],
                                            xm[:, k, :], start=(k == 0), stop=(k == DB - 1))
                last.then_inc(front_ready, 1)

            def dt_raw_proj(U, h, it):
                pe.wait_ge(w_x_in, 32 * (it // BATCH) + 32)
                pe.wait_ge(u_done, CB * U + 2 * CB)
                out = bank(U, DT_RAW)
                for k in range(CB):
                    last = nc.tensor.matmul(out[0:RANK, :], w_x_sb[:, k, 0:RANK], u[h][:, k, :],
                                            start=(k == 0), stop=(k == CB - 1))
                last.then_inc(front_ready, 1)

            def bc_proj(U, h):
                out = bank(U, BC_IN)
                for t in range(TC):
                    for k in range(CB):
                        last = nc.tensor.matmul(out[:, t * 2 * STATES:(t + 1) * 2 * STATES],
                                                u[h][:, k, t * P:(t + 1) * P], w_x_sb[:, k, RANK:],
                                                start=(k == 0), stop=(k == CB - 1))
                last.then_inc(front_ready, 1)

            def dt_proj(U, j):
                pe.wait_ge(front_act, act_reads(U, DT_RAW))
                out = bank(U, DT_IN + j)
                nc.tensor.matmul(out, w_dt_sb[:, j * P:(j + 1) * P], dt_raw[:], start=True, stop=True).then_inc(front_ready, 1)

            def turn_du(U, t):
                pe.wait_ge(delta_done, U + 2)
                out = bank(U, DU_T + t)
                for j in range(CB):
                    last = nc.tensor.transpose(out[:, j * P:(j + 1) * P], du[:, j, t * P:(t + 1) * P], ident[:])
                last.then_inc(front_ready, 1)

            def front(U, h, n, it, part):
                if n == 2 and part == 1:
                    in_proj(U, h, it, X_IN)
                if n in (3, 4, 5):
                    in_proj(U, h, it, X_IN + 1 + 2 * (n - 3) + part)
                if n == 6 and part == 0:
                    in_proj(U, h, it, Z_IN + CB - 1)
                if n == 9 and part == 0:
                    dt_raw_proj(U, h, it)
                if n == 9 and part == 1:
                    bc_proj(U, h)
                if n in (10, 11):
                    dt_proj(U, 2 * (n - 10) + part)
                if n in (15, 16):
                    turn_du(U, 2 * (n - 15) + part)

            def turn_duB(U, n, j):
                if j == 0:
                    pe.wait_ge(duB_done, U * STATES * TC + TC * n + TC)
                pe.wait_ge(scanned, SCAN_0 + U * STATES * CB + CB * n + j - 1)
                for t in range(TC):
                    last = nc.tensor.transpose(ps_b[:, j % 2, t * P:(t + 1) * P], duB[n % 2][:, t, j * P:(j + 1) * P], ident[:])
                last.then_inc(duB_turned, 1)

            def turn_state(U, n, t):
                if t == 0:
                    pe.wait_ge(scanned, SCAN_0 + U * STATES * CB + CB * n + CB)
                m, r = (n, t - 2) if t >= 2 else (n - 1, t + 2)
                if m < 0:
                    pe.wait_ge(yv_added, U * TC * NV + TC * (NV - 1) + r + 1)
                elif m in ON_VECTOR:
                    pe.wait_ge(yv_added, (U + 1) * TC * NV + TC * ON_VECTOR.index(m) + r + 1)
                else:
                    pe.wait_ge(prod_done, U * TC * NG + TC * ON_GPSIMD.index(m) + r + 1)
                for j in range(CB):
                    last = nc.tensor.transpose(ps_s[:, t % 2, j * P:(j + 1) * P], state[n % 2][:, j, t * P:(t + 1) * P], ident[:])
                last.then_inc(state_turned, 1)

            def turn_y(U, j, counts):
                pe.wait_ge(y_done, TC * U + 2 * TC)
                if j == 0:
                    pe.wait_ge(over_read, counts)
                pe.wait_ge(back_read, BACK_0 + BACK * U + j)
                for t in range(TC):
                    last = nc.tensor.transpose(ps_k[:, t * P:(t + 1) * P], yv[:, t, j * P:(j + 1) * P], ident[:])
                last.then_inc(back_ready, 1)

            def out_proj(U, it, k):
                pe.wait_ge(w_out_in, 16 * (it // BATCH) + 16)
                pe.wait_ge(gated_done, CB * U + CB)
                pe.wait_ge(back_read, BACK_0 + BACK * U + CB + k)
                for j in range(CB):
                    last = nc.tensor.matmul(ps_k[:], w_out_sb[:, j, k * P:(k + 1) * P], gated[:, j, :],
                                            start=(j == 0), stop=(j == CB - 1))
                last.then_inc(back_ready, 1)

            def unit(U, h, it, more):
                for n in range(STATES + 1):
                    for part in range(2):
                        j = 2 * part
                        if n < STATES:
                            turn_duB(U, n, j)
                        if n == 0 and h == 1 and part == 1:
                            turn_y(U - 1, 1, None)
                        if n < STATES:
                            turn_duB(U, n, j + 1)
                        if n == 0 and part == 0 and more:
                            count_over(U + 1, 1 - h)
                        if n == 0 and h == 1:
                            if part == 0:
                                turn_y(U - 1, 0, U + 2 if more else U + 1)
                            else:
                                turn_y(U - 1, 2, None)
                                turn_y(U - 1, 3, None)
                        if n in (1, 2) and part == 0 and h == 1:
                            out_proj(U - 1, it, n - 1)
                        if more:
                            front(U + 1, 1 - h, n, it + h, part)
                        if n:
                            turn_state(U, n - 1, j)
                            turn_state(U, n - 1, j + 1)
                if h == 1:
                    for j in range(CB):
                        turn_y(U, j, U + 2 if more else U + 1)
                    for k in range(DB):
                        out_proj(U, it, k)

            pe.sem_inc(duB_turned, DBU_0)
            pe.sem_inc(state_turned, HT_0)
            count_over(0, 0)
            for n in range(STATES + 1):
                for part in range(2):
                    front(0, 0, n, 0, part)
            units(pe, unit)


def experts(nc, x, xn_dram, alive_dram, wr, w1, b1, w2, b2, xres, ident, out):
    with ExitStack() as ctx:
        sb = lambda name, shape: ctx.enter_context(nc.sbuf_tensor(name, shape, F32))
        sem = lambda name: ctx.enter_context(nc.semaphore(name))
        STEPS = TOK // T
        HB, OB = 4, 4
        xn = sb("xn", [P, DB, TOK])
        wr_sb = sb("wr_sb", [P, DB, EXPERTS])
        w1_sb = [sb(f"w1_{e}", [P, DB, FF]) for e in range(2)]
        w2_sb = [sb(f"w2_{e}", [P, FB, D]) for e in range(2)]
        b1_sb = sb("b1_sb", [P, EXPERTS * FB])
        b2_sb = sb("b2_sb", [1, EXPERTS * D])
        ones = sb("ones", [1, P])
        hid = sb("hid", [P, FB, T])
        acc = sb("acc", [P, NTILE, D])
        route = [sb(f"route{i}", [P, NTILE, EXPERTS]) for i in range(2)]
        order = sb("order", [P, NTILE, EXPERTS])
        chosen = sb("chosen", [P, NTILE, EXPERTS])
        best = sb("best", [P, NTILE])
        total = sb("total", [P, NTILE])
        pmax = sb("pmax", [P, NTILE])
        alive_row = sb("alive_row", [NTILE, P])
        alive = sb("alive_t", [P, NTILE])
        xt = [sb(f"xt{i}", [P, TC, D]) for i in range(2)]
        clean = [sb(f"clean{i}", [P, DB, T]) for i in range(2)]
        valid = sb("valid", [P, DB, T])
        gate = [sb(f"gate{i}", [P, TC, D]) for i in range(2)]
        ps_h = ctx.enter_context(nc.psum_tensor("ps_h", [P, HB, T], F32))
        ps_o = ctx.enter_context(nc.psum_tensor("ps_o", [P, OB, 512], F32))
        small_in, xn_in, w_in, x_in, stored = sem("small_in"), sem("xn_in"), [sem("w0_in"), sem("w1_in")], [sem("x0_in"), sem("x1_in")], [sem("stored0"), sem("stored1")]
        ones_set, acc_set, order_set, routed, rs, rexp = sem("ones_set"), sem("acc_set"), sem("order_set"), sem("routed"), sem("rs"), sem("rexp")
        hid_ready, hid_set, out_ready, acc_added = sem("hid_ready"), sem("hid_set"), sem("out_ready"), sem("acc_added")
        cleaned, cstep, s_turned, gate_set, final = sem("cleaned"), sem("cstep"), sem("s_turned"), sem("gate_set"), sem("final")
        block = ctx.enter_context(nc.Block())
        x_v = x.rearrange("(s i p) d -> s p i d", i=TC, p=P)
        out_v = out.rearrange("(s i p) d -> s p i d", i=TC, p=P)

        @block.sync
        def _(sp):
            sp.dma_start(xn[:], xn_dram).then_inc(xn_in, 16)
            sp.dma_start(wr_sb[:], wr).then_inc(small_in, 16)
            sp.dma_start(alive_row[:], alive_dram.rearrange("a (i p) -> (a i) p", p=P)).then_inc(small_in, 16)
            sp.dma_start(b1_sb[:], b1).then_inc(small_in, 16)
            sp.dma_start(b2_sb[:], b2).then_inc(small_in, 16)

            def load(pair, e):
                sp.dma_start(w1_sb[e][:], w1[:, :, bass.ds((2 * pair + e) * FF, FF)]).then_inc(w_in[e], 16)
                sp.dma_start(w2_sb[e][:], w2[:, :, bass.ds((2 * pair + e) * D, D)]).then_inc(w_in[e], 16)

            load(0, 0)
            load(0, 1)
            with sp.Fori(1, EXPERTS // 2) as pair:
                for e in range(2):
                    sp.wait_ge(out_ready, (2 * pair + e - 1) * STEPS * TC)
                    load(pair, e)
            for s in range(STEPS):
                if s >= 2:
                    sp.wait_ge(final, s - 1)
                sp.dma_start(xt[s % 2][:], x_v[s]).then_inc(x_in[s % 2], 16)
                if s:
                    sp.wait_ge(final, s)
                    sp.dma_start(out_v[s - 1], gate[(s - 1) % 2][:]).then_inc(stored[(s - 1) % 2], 16)
            sp.wait_ge(final, STEPS)
            sp.dma_start(out_v[STEPS - 1], gate[(STEPS - 1) % 2][:]).then_inc(stored[(STEPS - 1) % 2], 16)
            for i in range(2):
                sp.wait_ge(stored[i], 16 * STEPS // 2)

        @block.gpsimd
        def _(pool):
            nc.gpsimd.memset(ones[:], 1.0).then_inc(ones_set, 1)
            nc.gpsimd.memset(acc[:], 0.0).then_inc(acc_set, 1)
            for e in range(EXPERTS):
                nc.gpsimd.memset(order[:, :, e:e + 1], float(EXPERTS - e)).then_inc(order_set, 1)

        @block.tensor
        def _(pe):
            pe.wait_ge(xn_in, 16)
            pe.wait_ge(small_in, 64)
            pe.wait_ge(ones_set, 1)
            for i in range(NTILE):
                for k in range(DB):
                    last = nc.tensor.matmul(ps_o[:, 0, i * EXPERTS:(i + 1) * EXPERTS], xn[:, k, i * P:(i + 1) * P],
                                            wr_sb[:, k, :], start=(k == 0), stop=(k == DB - 1))
            last = nc.tensor.transpose(ps_o[:, 1, 0:NTILE], alive_row[:], ident[0:NTILE, 0:NTILE])
            last.then_inc(routed, 1)
            pe.wait_ge(rs, 1)
            with pe.Fori(0, EXPERTS // 2) as pair:
                for e in range(2):
                    with pe.Fori(0, STEPS) as s:
                        pe.wait_ge(w_in[e], 32 * pair + 32)
                        g = (2 * pair + e) * STEPS + s
                        for f in range(FB):
                            pe.wait_ge(hid_set, FB * g + f + 1)
                            for k in range(DB):
                                last = nc.tensor.matmul(ps_h[:, f % HB, :], w1_sb[e][:, k, f * P:(f + 1) * P],
                                                        xn[:, k, bass.ds(s * T, T)], start=(k == 0), stop=(k == DB - 1))
                            last.then_inc(hid_ready, 1)
                        pe.wait_ge(hid_set, FB * g + FB + HB)
                        for i in range(TC):
                            pe.wait_ge(acc_added, TC * g + i + 1 + ACC_0 - OB)
                            for f in range(FB):
                                nc.tensor.matmul(ps_o[:, i, 0:D], hid[:, f, i * P:(i + 1) * P], w2_sb[e][:, f, :],
                                                 start=(f == 0), stop=False)
                            nc.tensor.matmul(ps_o[:, i, 0:D], ones[:], b2_sb[:, bass.ds((2 * pair + e) * D, D)],
                                             start=False, stop=True).then_inc(out_ready, 1)
            for s in range(STEPS):
                pe.wait_ge(cleaned, s + 1)
                pe.wait_ge(hid_set, FB * EXPERTS * STEPS + HB)
                if s >= 2:
                    pe.wait_ge(final, s - 1)
                for i in range(TC):
                    for k in range(DB):
                        c = (i % 2) * D + k * P
                        last = nc.tensor.transpose(ps_h[:, (s % 2) * 2 + i // 2, c:c + P],
                                                   clean[s % 2][:, k, i * P:(i + 1) * P], ident[:])
                last.then_inc(s_turned, 1)

        @block.scalar
        def _(act):
            act.wait_ge(rs, 1)
            nc.scalar.activation(route[0][:], route[0][:], ACT.Exp).then_inc(rexp, 1)
            act.wait_ge(small_in, 64)
            act.sem_inc(hid_set, HB)
            with act.Fori(0, EXPERTS) as e:
                with act.Fori(0, STEPS) as s:
                    for f in range(FB):
                        act.wait_ge(hid_ready, (e * STEPS + s) * FB + f + 1)
                        nc.scalar.activation(hid[:, f, :], ps_h[:, f % HB, :], ACT.Gelu,
                                             bias=b1_sb[:, bass.ds(e * FB + f, 1)]).then_inc(hid_set, 1)
            act.wait_ge(acc_added, ACC_0 + EXPERTS * NTILE)
            act.wait_ge(rs, ROUTE_STEPS)
            for s in range(STEPS):
                if s >= 2:
                    act.wait_ge(stored[s % 2], 16 * (s // 2))
                for i in range(TC):
                    t = s * TC + i
                    nc.scalar.activation(gate[s % 2][:, i, :], acc[:, t, :], ACT.Silu, scale=pmax[:, t:t + 1]).then_inc(gate_set, 1)

        @block.vector
        def _(dve):
            over = lambda a: a[:].unsqueeze(2).to_broadcast([P, NTILE, EXPERTS])
            logits = ps_o[:, 0, 0:NTILE * EXPERTS].rearrange("p (i e) -> p i e", e=EXPERTS)
            dve.wait_ge(routed, 1)
            nc.vector.tensor_copy(alive[:], ps_o[:, 1, 0:NTILE])
            nc.vector.tensor_reduce(best[:], logits, AX_X, ALU.max).then_inc(cstep, 1)
            dve.wait_ge(cstep, 1)
            nc.vector.tensor_tensor(route[0][:], logits, over(best), ALU.subtract).then_inc(rs, 1)
            dve.wait_ge(rexp, 1)
            nc.vector.tensor_reduce(total[:], route[0][:], AX_X, ALU.add).then_inc(rs, 1)
            dve.wait_ge(rs, 2)
            nc.vector.reciprocal(total[:], total[:]).then_inc(rs, 1)
            dve.wait_ge(rs, 3)
            nc.vector.tensor_tensor(route[0][:], route[0][:], over(total), ALU.mult).then_inc(rs, 1)
            dve.wait_ge(rs, 4)
            nc.vector.tensor_reduce(pmax[:], route[0][:], AX_X, ALU.max).then_inc(rs, 1)
            dve.wait_ge(rs, 5)
            nc.vector.tensor_tensor(route[1][:], route[0][:], over(pmax), ALU.is_ge).then_inc(rs, 1)
            dve.wait_ge(rs, 6)
            dve.wait_ge(order_set, EXPERTS)
            nc.vector.tensor_tensor(route[1][:], route[1][:], order[:], ALU.mult).then_inc(rs, 1)
            dve.wait_ge(rs, 7)
            nc.vector.tensor_reduce(best[:], route[1][:], AX_X, ALU.max).then_inc(rs, 1)
            dve.wait_ge(rs, 8)
            nc.vector.tensor_tensor(chosen[:], route[1][:], over(best), ALU.is_equal).then_inc(rs, 1)
            dve.wait_ge(small_in, 64)
            nc.vector.tensor_tensor(pmax[:], pmax[:], alive[:], ALU.mult).then_inc(rs, 1)
            dve.wait_ge(rs, ROUTE_STEPS)
            dve.wait_ge(acc_set, 1)
            dve.sem_inc(acc_added, ACC_0)
            with dve.Fori(0, EXPERTS) as e:
                with dve.Fori(0, STEPS) as s:
                    for i in range(TC):
                        a = acc[:, bass.ds(s * TC + i, 1), :].rearrange("p a d -> p (a d)")
                        dve.wait_ge(out_ready, (e * STEPS + s) * TC + i + 1)
                        dve.wait_ge(acc_added, (e * STEPS + s) * TC + i + 1)
                        nc.vector.scalar_tensor_tensor(
                            a, ps_o[:, i, 0:D], chosen[:, bass.ds(s * TC + i, 1), bass.ds(e, 1)].rearrange("p a e -> p (a e)"),
                            a, ALU.mult, ALU.add).then_inc(acc_added, 1)

            def clean_up(s):
                src = xres[:, :, s * T:(s + 1) * T]
                if s:
                    dve.wait_ge(cleaned, s)
                nc.vector.tensor_tensor(valid[:], src, src, ALU.is_equal)
                if s >= 2:
                    dve.wait_ge(s_turned, s - 1)
                nc.vector.tensor_scalar(clean[s % 2][:], src, -FLT_MAX, FLT_MAX, ALU.max, ALU.min).then_inc(cstep, 1)
                dve.wait_ge(cstep, s + 2 + max(s - 1, 0))
                nc.vector.tensor_tensor(clean[s % 2][:], clean[s % 2][:], valid[:], ALU.mult).then_inc(cleaned, 1)

            clean_up(0)
            for s in range(STEPS):
                if s + 1 < STEPS:
                    clean_up(s + 1)
                dve.wait_ge(s_turned, s + 1)
                dve.wait_ge(gate_set, TC * (s + 1))
                flat = lambda a: a[:].rearrange("p i d -> p (i d)")
                nc.vector.tensor_tensor(flat(gate[s % 2]), flat(gate[s % 2]),
                                        ps_h[:, (s % 2) * 2:(s % 2) * 2 + 2, :].rearrange("p b c -> p (b c)"),
                                        ALU.mult).then_inc(cstep, 1)
                dve.wait_ge(cstep, min(s + 2, STEPS) + s + 2)
                dve.wait_ge(x_in[s % 2], 16 * (s // 2 + 1))
                nc.vector.tensor_tensor(gate[s % 2][:], gate[s % 2][:], xt[s % 2][:], ALU.add).then_inc(final, 1)


ACC_0 = NTILE
ROUTE_STEPS = 10


def program(nc, x, w_in, w_x, w_dt, w_out, par, wr, w1, b1, w2, b2, xn_dram, alive_dram, out):
    with ExitStack() as ctx:
        xres = ctx.enter_context(nc.sbuf_tensor("xres", [P, DB, TOK], F32))
        ident = ctx.enter_context(nc.sbuf_tensor("ident", [P, P], F32))
        normalise(nc, x, xn_dram, xres, ident)
        mamba(nc, w_in, w_x, w_dt, w_out, par, xres, ident, alive_dram)
        experts(nc, x, xn_dram, alive_dram, wr, w1, b1, w2, b2, xres, ident, out)


def kernel(**inputs):
    import concourse.bacc as bacc
    from concourse.bass_utils import run_bass_kernel_spmd

    a = {name.removeprefix("L0_"): np.asarray(v) for name, v in inputs.items()}

    def blocks(w, n):
        w = w.reshape(w.shape[:-2] + (n, P, w.shape[-1]))
        w = w[None] if w.ndim == 3 else w
        return np.ascontiguousarray(w.transpose(2, 1, 0, 3).reshape(P, n, -1))

    by_channel = lambda v: v.reshape(LAYERS, CB, P, -1).transpose(2, 0, 1, 3).reshape(P, LAYERS, -1)
    arrays = {
        "x": a["attn_x"].reshape(TOK, D),
        "w_in": blocks(a["attn_W_in"].transpose(0, 2, 1), DB),
        "w_x": blocks(a["attn_W_x"].transpose(0, 2, 1), CB),
        "w_dt": a["attn_W_dt"].transpose(2, 0, 1).reshape(RANK, LAYERS * INNER),
        "w_out": blocks(a["attn_W_out"].transpose(0, 2, 1), CB),
        "par": np.concatenate([by_channel(a["attn_" + n]) for n in ("A_log", "conv_w", "conv_b", "b_dt", "D_par")], axis=2),
        "wr": blocks(a["ffn_Wr"], DB),
        "w1": blocks(a["ffn_W1"], DB),
        "b1": a["ffn_b1"].reshape(EXPERTS * FB, P).T,
        "w2": blocks(a["ffn_W2"], FB),
        "b2": a["ffn_b2"].reshape(1, EXPERTS * D),
    }
    arrays = {name: np.ascontiguousarray(v) for name, v in arrays.items()}
    nc = bacc.Bacc("TRN2", target_bir_lowering=False, num_devices=1)
    args = [nc.dram_tensor(name, v.shape, F32, kind="ExternalInput").ap() for name, v in arrays.items()]
    args.append(nc.dram_tensor("xn_dram", (P, DB, TOK), F32, kind="Internal").ap())
    args.append(nc.dram_tensor("alive_dram", (1, TOK), F32, kind="Internal").ap())
    args.append(nc.dram_tensor("out", (TOK, D), F32, kind="ExternalOutput").ap())
    program(nc, *args)
    got = run_bass_kernel_spmd(nc, [arrays], core_ids=[0])
    return got.results[0]["out"].reshape(BATCH, SEQ, D)
```
